# Optimizing a Trainium2 kernel written in Bass

```python
import numpy as np
import jax
import jax.numpy as jnp

def _softmax(x, axis=-1):
    return jax.nn.softmax(x, axis=axis)

def _gelu(x):
    return jax.nn.gelu(x, approximate=True)

def _silu(x):
    return jax.nn.silu(x)

def _sigmoid(x):
    return jax.nn.sigmoid(x)

def _layernorm(x, axis=-1, eps=1e-05):
    m = jnp.mean(x, axis=axis, keepdims=True)
    v = jnp.var(x, axis=axis, keepdims=True)
    return (x - m) / jnp.sqrt(v + eps)

def _scatter_add(tgt, idx, src, axis=0):
    return tgt.at[idx].add(src)

def _segment_sum(src, seg, n):
    return jax.ops.segment_sum(src, seg, n)
kernel_name = 'mk_gnn_resnorm_d4_gnn_r8_66909f'

def setup_inputs(seed: int=0):
    np.random.seed(seed)
    _w = jnp.asarray

    def _rec_inputs():
        import jax
        import jax.numpy as jnp
        _gk = jax.random.key(seed)
        x = -0.0002117 + 1 * jax.random.normal(jax.random.fold_in(_gk, 1), (1250, 512), jnp.float32)
        src = jax.random.randint(jax.random.fold_in(_gk, 2), (20000,), 0, 1250, jnp.int32)
        dst = jax.random.randint(jax.random.fold_in(_gk, 3), (20000,), 0, 1250, jnp.int32)
        _o = jnp.argsort(dst, stable=True)
        src = src[_o]
        dst = dst[_o]
        edge_attr_8 = 0.0012443 + 1.0001 * jax.random.normal(jax.random.fold_in(_gk, 11), (20000, 8), jnp.float32)
        edge_type_2 = jax.random.randint(jax.random.fold_in(_gk, 13), (20000,), 0, 2, jnp.int32)
        edge_weight = jax.random.uniform(jax.random.fold_in(_gk, 14), (20000,), jnp.float32, 0.0, 0.999999)
        return (x, src, dst, edge_attr_8, edge_type_2, edge_weight)
    x, src, dst, edge_attr_8, edge_type_2, edge_weight = _rec_inputs()

    def _L0_gnn_setup():
        import jax, jax.numpy as jnp
        import numpy as np
        N_NODES = 6250
        N_EDGES = 200000
        IN_F = 512
        OUT_F = 512
        key = jax.random.key(seed)
        k1, k2, k3, k4, k5 = jax.random.split(key, 5)
        input = jax.random.normal(k1, (N_NODES, IN_F), dtype=jnp.float32)
        edge_index = jax.random.randint(k2, (2, N_EDGES), 0, N_NODES, dtype=jnp.int64)
        edge_vals = jax.random.uniform(k3, (N_EDGES,), dtype=jnp.float32)
        stdv = 1.0 / np.sqrt(OUT_F)
        weight = jax.random.uniform(k4, (IN_F, OUT_F), dtype=jnp.float32, minval=-stdv, maxval=stdv)
        bias = jax.random.uniform(k5, (OUT_F,), dtype=jnp.float32, minval=-stdv, maxval=stdv)
        return {'input': input, 'edge_index': edge_index, 'edge_vals': edge_vals, 'weight': weight, 'bias': bias}
    _L0_gnn_all = _L0_gnn_setup()
    _L0_gnn_in = {k: v for k, v in _L0_gnn_all.items() if k in ('weight', 'bias')}
    del _L0_gnn_all

    def _L1_gnn_setup():
        import jax, jax.numpy as jnp
        import numpy as np
        NUM_RELATIONS = 2
        NUM_BASES = 30
        HIDDEN = 512
        N_NODES = 1250
        N_EDGES = 20000

        def rgcn_gate_layer(x, row, col, edge_type, basis, att, gate_w, root, bias):
            H = x.shape[1]
            w = jnp.einsum('rb,bio->rio', att, basis)
            x_j = x[col]
            msgs = []
            for r in range(NUM_RELATIONS):
                gate = jax.nn.sigmoid(x_j @ gate_w[r, :, 0])
                msgs.append(gate[:, None] * x_j @ w[r])
            msg = jnp.where((edge_type == 0)[:, None], msgs[0], msgs[1])
            agg = jax.ops.segment_sum(msg, row, num_segments=x.shape[0])
            return agg + x @ root + bias
        key = jax.random.key(seed)
        ks = jax.random.split(key, 16)
        H, R, B = (HIDDEN, NUM_RELATIONS, NUM_BASES)
        bound = 1.0 / np.sqrt(B * H)
        u = lambda k, shape: jax.random.uniform(k, shape, jnp.float32, -bound, bound)
        inp = {'x': jax.random.normal(ks[0], (N_NODES, H), jnp.float32), 'edge_index': jax.random.randint(ks[1], (2, N_EDGES), 0, N_NODES, jnp.int32), 'edge_type': jax.random.randint(ks[2], (N_EDGES,), 0, R, jnp.int32), 'basis1': u(ks[3], (B, H, H)), 'att1': u(ks[4], (R, B)), 'gate_w1': u(ks[5], (R, H, 1)), 'root1': u(ks[6], (H, H)), 'bias1': u(ks[7], (H,)), 'basis2': u(ks[8], (B, H, H)), 'att2': u(ks[9], (R, B)), 'gate_w2': u(ks[10], (R, H, 1)), 'root2': u(ks[11], (H, H)), 'bias2': u(ks[12], (H,))}
        return inp
    _L1_gnn_all = _L1_gnn_setup()
    _L1_gnn_in = {k: v for k, v in _L1_gnn_all.items() if k in ('basis1', 'att1', 'gate_w1', 'root1', 'bias1', 'basis2', 'att2', 'gate_w2', 'root2', 'bias2')}
    del _L1_gnn_all

    def _L2_gnn_setup():
        import jax, jax.numpy as jnp
        import numpy as np
        NUM_NODES = 6250
        NUM_EDGES = 200000
        IN_C = 512
        OUT_C = 512
        key = jax.random.key(seed)
        k1, k2, k3, k4 = jax.random.split(key, 4)
        x = jax.random.normal(k1, (NUM_NODES, IN_C), dtype=jnp.float32)
        edge_index = jax.random.randint(k2, (2, NUM_EDGES), 0, NUM_NODES, dtype=jnp.int64)
        lim = 1.0 / np.sqrt(IN_C)
        W = jax.random.uniform(k3, (OUT_C, IN_C), dtype=jnp.float32, minval=-lim, maxval=lim)
        b = jax.random.uniform(k4, (OUT_C,), dtype=jnp.float32, minval=-lim, maxval=lim)
        return {'x': x, 'edge_index': edge_index, 'W': W, 'b': b}
    _L2_gnn_all = _L2_gnn_setup()
    _L2_gnn_in = {k: v for k, v in _L2_gnn_all.items() if k in ('W', 'b')}
    del _L2_gnn_all

    def _L3_gnn_setup():
        import jax, jax.numpy as jnp
        import numpy as np
        N = 2500
        E = 40000
        D = 512
        H = 8
        DK = D // H
        key = jax.random.key(seed)
        ks = jax.random.split(key, 12)
        x = jax.random.normal(ks[0], (N, D), jnp.float32)
        rows = jnp.sort(jax.random.randint(ks[1], (E,), 0, N))
        cols = jax.random.randint(ks[2], (E,), 0, N)
        edge_index = jnp.stack([rows, cols]).astype(jnp.int32)
        att_bias = jax.random.normal(ks[3], (E, H), jnp.float32)
        s = float(1.0 / np.sqrt(D))
        Wq = jax.random.normal(ks[4], (D, D), jnp.float32) * s
        Wk = jax.random.normal(ks[5], (D, D), jnp.float32) * s
        Wv = jax.random.normal(ks[6], (D, D), jnp.float32) * s
        Wo = jax.random.normal(ks[7], (D, D), jnp.float32) * s
        bq = jnp.zeros((D,), jnp.float32)
        bk = jnp.zeros((D,), jnp.float32)
        bv = jnp.zeros((D,), jnp.float32)
        bo = jnp.zeros((D,), jnp.float32)
        return dict(x=x, edge_index=edge_index, att_bias=att_bias, Wq=Wq, bq=bq, Wk=Wk, bk=bk, Wv=Wv, bv=bv, Wo=Wo, bo=bo)
    _L3_gnn_all = _L3_gnn_setup()
    _L3_gnn_in = {k: v for k, v in _L3_gnn_all.items() if k in ('Wq', 'bq', 'Wk', 'bk', 'Wv', 'bv', 'Wo', 'bo')}
    del _L3_gnn_all
    return {'x': x, 'src': src, 'dst': dst, 'edge_attr_8': edge_attr_8, 'edge_type_2': edge_type_2, 'edge_weight': edge_weight, 'L0_gnn_weight': _L0_gnn_in['weight'], 'L0_gnn_bias': _L0_gnn_in['bias'], 'L1_gnn_basis1': _L1_gnn_in['basis1'], 'L1_gnn_att1': _L1_gnn_in['att1'], 'L1_gnn_gate_w1': _L1_gnn_in['gate_w1'], 'L1_gnn_root1': _L1_gnn_in['root1'], 'L1_gnn_bias1': _L1_gnn_in['bias1'], 'L1_gnn_basis2': _L1_gnn_in['basis2'], 'L1_gnn_att2': _L1_gnn_in['att2'], 'L1_gnn_gate_w2': _L1_gnn_in['gate_w2'], 'L1_gnn_root2': _L1_gnn_in['root2'], 'L1_gnn_bias2': _L1_gnn_in['bias2'], 'L2_gnn_W': _L2_gnn_in['W'], 'L2_gnn_b': _L2_gnn_in['b'], 'L3_gnn_Wq': _L3_gnn_in['Wq'], 'L3_gnn_bq': _L3_gnn_in['bq'], 'L3_gnn_Wk': _L3_gnn_in['Wk'], 'L3_gnn_bk': _L3_gnn_in['bk'], 'L3_gnn_Wv': _L3_gnn_in['Wv'], 'L3_gnn_bv': _L3_gnn_in['bv'], 'L3_gnn_Wo': _L3_gnn_in['Wo'], 'L3_gnn_bo': _L3_gnn_in['bo']}

def reference(x, src, dst, edge_attr_8, edge_type_2, edge_weight, L0_gnn_weight, L0_gnn_bias, L1_gnn_basis1, L1_gnn_att1, L1_gnn_gate_w1, L1_gnn_root1, L1_gnn_bias1, L1_gnn_basis2, L1_gnn_att2, L1_gnn_gate_w2, L1_gnn_root2, L1_gnn_bias2, L2_gnn_W, L2_gnn_b, L3_gnn_Wq, L3_gnn_bq, L3_gnn_Wk, L3_gnn_bk, L3_gnn_Wv, L3_gnn_bv, L3_gnn_Wo, L3_gnn_bo):
    import jax
    import jax.numpy as jnp

    def _L0_gnn_ref(input, edge_index, edge_vals, weight, bias):
        import jax, jax.numpy as jnp
        import numpy as np
        N_NODES = 6250
        N_EDGES = 200000
        IN_F = 512
        OUT_F = 512
        support = jnp.matmul(input, weight)
        dst, src = (edge_index[0], edge_index[1])
        messages = support[src] * edge_vals[:, None]
        output = jax.ops.segment_sum(messages, dst, num_segments=input.shape[0])
        return output + bias

    def _L1_gnn_ref(x, edge_index, edge_type, basis1, att1, gate_w1, root1, bias1, basis2, att2, gate_w2, root2, bias2):
        import jax, jax.numpy as jnp
        import numpy as np
        NUM_RELATIONS = 2
        NUM_BASES = 30
        HIDDEN = 512
        N_NODES = 1250
        N_EDGES = 20000

        def rgcn_gate_layer(x, row, col, edge_type, basis, att, gate_w, root, bias):
            H = x.shape[1]
            w = jnp.einsum('rb,bio->rio', att, basis)
            x_j = x[col]
            msgs = []
            for r in range(NUM_RELATIONS):
                gate = jax.nn.sigmoid(x_j @ gate_w[r, :, 0])
                msgs.append(gate[:, None] * x_j @ w[r])
            msg = jnp.where((edge_type == 0)[:, None], msgs[0], msgs[1])
            agg = jax.ops.segment_sum(msg, row, num_segments=x.shape[0])
            return agg + x @ root + bias
        row, col = (edge_index[0], edge_index[1])
        h = jax.nn.relu(rgcn_gate_layer(x, row, col, edge_type, basis1, att1, gate_w1, root1, bias1))
        out = rgcn_gate_layer(h, row, col, edge_type, basis2, att2, gate_w2, root2, bias2)
        return out

    def _L2_gnn_ref(x, edge_index, W, b):
        import jax, jax.numpy as jnp
        import numpy as np
        NUM_NODES = 6250
        NUM_EDGES = 200000
        IN_C = 512
        OUT_C = 512
        num_nodes = x.shape[0]
        src = edge_index[0]
        tar = edge_index[1]
        feat = jnp.einsum('ni,oi->no', x, W) + b
        ones_e = jnp.ones((src.shape[0],), dtype=feat.dtype)
        deg = jax.ops.segment_sum(ones_e, src, num_segments=num_nodes) + 1.0
        deg_inv_sqrt = jnp.where(deg > 0, deg ** (-0.5), 0.0)
        w = deg_inv_sqrt[src] * deg_inv_sqrt[tar]
        msgs = w[:, None] * feat[tar]
        out = jax.ops.segment_sum(msgs, src, num_segments=num_nodes)
        out = out + feat * (1.0 / deg)[:, None]
        return out

    def _L3_gnn_ref(x, edge_index, att_bias, Wq, bq, Wk, bk, Wv, bv, Wo, bo):
        import jax, jax.numpy as jnp
        import numpy as np
        N = 2500
        E = 40000
        D = 512
        H = 8
        DK = D // H
        n = x.shape[0]
        rows, cols = (edge_index[0], edge_index[1])
        q = (x @ Wq + bq).reshape(n, H, DK)
        k = (x @ Wk + bk).reshape(n, H, DK)
        v = (x @ Wv + bv).reshape(n, H, DK)
        scale = 1.0 / jnp.sqrt(jnp.asarray(DK, x.dtype))
        logits = jnp.einsum('ehd,ehd->eh', q[rows] * scale, k[cols]) + att_bias
        row_max = jax.ops.segment_max(logits, rows, num_segments=n)
        p = jnp.exp(logits - row_max[rows])
        denom = jax.ops.segment_sum(p, rows, num_segments=n)
        att = p / denom[rows]
        y = jax.ops.segment_sum(att[:, :, None] * v[cols], rows, num_segments=n)
        out = y.reshape(n, H * DK) @ Wo + bo
        return out
    edge_index = jnp.stack([src, dst])
    x = _layernorm(x + _L0_gnn_ref(x, edge_index, edge_weight, L0_gnn_weight, L0_gnn_bias), axis=-1)
    x = _layernorm(x + _L1_gnn_ref(x, edge_index, edge_type_2, L1_gnn_basis1, L1_gnn_att1, L1_gnn_gate_w1, L1_gnn_root1, L1_gnn_bias1, L1_gnn_basis2, L1_gnn_att2, L1_gnn_gate_w2, L1_gnn_root2, L1_gnn_bias2), axis=-1)
    x = _layernorm(x + _L2_gnn_ref(x, edge_index, L2_gnn_W, L2_gnn_b), axis=-1)
    x = _layernorm(x + _L3_gnn_ref(x, edge_index, edge_attr_8, L3_gnn_Wq, L3_gnn_bq, L3_gnn_Wk, L3_gnn_bk, L3_gnn_Wv, L3_gnn_bv, L3_gnn_Wo, L3_gnn_bo), axis=-1)
    return x

_drawn_inputs = setup_inputs


def setup_inputs(seed=0):
    import zlib

    import numpy as np

    out = dict(_drawn_inputs(seed))
    spreads = {'L3_gnn_bq': (0.0, 0.281),
     'L3_gnn_bk': (0.0, 0.8),
     'L3_gnn_bv': (0.0, 0.1),
     'L3_gnn_bo': (0.0, 0.1)}
    factors = {'L1_gnn_basis1': 8.0,
     'L1_gnn_att1': 8.0,
     'L1_gnn_gate_w1': 8.0,
     'L1_gnn_root1': 8.0,
     'L1_gnn_bias1': 8.0,
     'L1_gnn_basis2': 8.0,
     'L1_gnn_att2': 8.0,
     'L1_gnn_gate_w2': 8.0,
     'L1_gnn_root2': 5.854,
     'L1_gnn_bias2': 8.0}
    for name, (base, spread) in spreads.items():
        noise = np.random.default_rng([zlib.crc32(name.encode()), seed]).standard_normal(out[name].shape)
        drawn = base * np.exp(spread * noise) if base else spread * noise
        out[name] = jnp.asarray(drawn.astype(out[name].dtype))
    for name, factor in factors.items():
        out[name] = (out[name] * factor).astype(out[name].dtype)
    return out
```

```python
from contextlib import ExitStack

import concourse.bass as bass
from concourse import mybir

F32 = mybir.dt.float32
F16 = mybir.dt.float16
BF16 = mybir.dt.bfloat16
I32 = mybir.dt.int32
ALU = mybir.AluOpType
ACT = mybir.ActivationFunctionType
AX = mybir.AxisListType

P = 128
NODES = 1250
NT = -(-NODES // P)
NN = NT * P
D = 512
FT = D // P
EDGES = 20000
EC = 125
CH = EDGES // EC
HALF = CH // 2
HEADS = 8
DK = D // HEADS
BASES = 30
BJ = BASES * FT
RELS = 2
EPS = 1e-5
ROWB = 320
NROWB = NN // ROWB
CW = 10
TT = NN // CW
MA = 4
MB = CW * HEADS
MH = MB + CW * MA
PIECES = [(0, 512), (512, 1024), (1024, NN)]
HOTS = 8
BIG = 1e30
MSCALE = 64.0
LAST = NODES - (NT - 1) * P


def gnn_resnorm(nc, a, out):
    ctx = ExitStack()
    with ctx:
        def sb(name, shape, dt):
            return ctx.enter_context(nc.sbuf_tensor(name, shape, dt))

        def sem(name):
            return ctx.enter_context(nc.semaphore(name))

        def dram(name, shape, dt):
            return nc.dram_tensor(name, shape, dt, kind="Internal").ap()

        adj_d = dram("adj_d", (NN * MA, NN), F32)
        bias_d = dram("bias_d", (NN * HEADS, NN), F32)
        w_d = [dram(f"w_d{i}", (RELS * FT, P, D), F32) for i in range(2)]
        tab_d = dram("tab_d", (1, TT), I32)
        x1_d = dram("x1_d", (P, NT * D), F32)
        max_d = dram("max_d", (NT * HEADS, P), F16)
        den_d = dram("den_d", (HEADS, NN), F32)
        rden_d = dram("rden_d", (HEADS, NN), F32)

        XX = sb("XX", [P, NT * D + FT * NN], F32)
        X = XX[:, 0:NT * D].rearrange("p (k f) -> p k f", k=NT)
        XT = XX[:, NT * D:].rearrange("p (f n) -> p f n", f=FT)
        R1 = sb("R1", [P, 2 * NT * NN], F16)
        R2 = sb("R2", [P, NT * NN], F32)
        R3 = sb("R3", [P, RELS * FT * NN], F32)
        W = sb("W", [P, 3, FT, D], F32)
        ident = sb("ident", [P, P], F32)
        ident16 = sb("ident16", [P, P], F16)
        ones = sb("ones", [P, P], F32)
        brow = sb("brow", [1, D], F32)
        stat = sb("stat", [P, 16], F32)
        gw = sb("gw", [P, 2, FT, RELS], F32)
        gw16 = sb("gw16", [P, 2, 2, FT, RELS], F16)
        gate = sb("gate", [P, NT, RELS], F32)
        dis = sb("dis", [P, NT], F32)
        degs = sb("degs", [P, NT], F32)
        dis16 = sb("dis16", [P, 2, NT], F16)
        one16 = sb("one16", [P, 1], F16)
        qkb = sb("qkb", [DK, 2, HEADS], F32)
        pidx = sb("pidx", [P, 1], F32)

        w_b = W[:, :, :, :].rearrange("p a b c -> p (a b c)")
        r1 = R1[:, :]
        r2 = R2[:, :]
        r3 = R3[:, :]

        base = XX[:, 0:TT].rearrange("p (t u) -> p t u", u=4)
        ownH = XX[:, TT:TT + CH * MH // 2].bitcast(F16).rearrange("p (c m) -> p c m", c=CH)
        o = NT * NN - CH * MB // 2
        ownL = r2[:, o:o + CH * MB // 2].bitcast(F16).rearrange("p (c m) -> p c m", c=CH)
        hot = r2[:, 0:HOTS * NN // 2].bitcast(F16).rearrange("p (s r) -> p s r", s=HOTS)
        o = 0
        eq = r2[:, o:o + CH * CW // 2].bitcast(F16).rearrange("p (c w) -> p c w", c=CH)
        o += CH * CW // 2
        valBh = r2[:, o:o + CH * 4].bitcast(F16).rearrange("p (c m) -> p c m", m=HEADS)
        o += CH * 4
        valBl = r2[:, o:o + CH * 4].bitcast(F16).rearrange("p (c m) -> p c m", m=HEADS)
        o += CH * 4
        valA = r2[:, o:o + CH * 2].bitcast(F16).rearrange("p (c m) -> p c m", m=MA)
        o += CH * 2
        assert max(o, HOTS * NN // 2) + CH * MB // 2 <= NT * NN
        key = w_b[:, 0:CH]
        o = CH
        basis = w_b[:, o:o + 2 * 4 * D].rearrange("p (s t n) -> p s t n", s=2, t=4)
        o += 2 * 4 * D
        attbd = w_b[:, o:o + 2 * RELS * FT].rearrange("p (l r j) -> p l r j", l=2, r=RELS)
        o += 2 * RELS * FT
        assert o <= 3 * FT * D
        stage = r3[:, 0:4 * NN].rearrange("p (s r) -> p s r", s=4)
        adjin = r3[:, 4 * NN:8 * NN].rearrange("p (s m r) -> p s m r", s=2, m=2)
        o = 6 * NN
        wst = r3[:, o:o + 2 * D].rearrange("p (h n) -> p h n", h=2)
        o += 2 * D
        iota16 = r3[:, o:o + NN // 2].bitcast(F16)
        o += NN // 2
        tab = r3[0:1, o:o + TT].bitcast(I32)
        o += TT
        assert o <= RELS * FT * NN
        o = 0

        def tmp(n):
            nonlocal o
            o += n
            assert o <= 6 * NN
            return r3[:, o - n:o]

        src_i = tmp(CH).bitcast(I32)
        dst_i = tmp(CH).bitcast(I32)
        typ_i = tmp(CH).bitcast(I32)
        wgt = tmp(CH)
        attr = tmp(CH * HEADS).rearrange("p (c h) -> p c h", h=HEADS)
        dcm_i = tmp(2 * EC).bitcast(I32).rearrange("p (g e) -> p g e", g=2)
        dcm = tmp(2 * EC).rearrange("p (g e) -> p g e", g=2)
        ext = tmp(4)
        diag4 = tmp(4 * HALF).rearrange("p (q c) -> p q c", q=4)
        crow = tmp(4 * HALF)
        ramp = tmp(CH)
        inside = tmp(CH)
        cond = tmp(CH)
        val = tmp(CH)
        bound = tmp(2)
        lohi = tmp(2)
        tabi = tmp(3).bitcast(I32)
        upper = tmp(TT)
        bmax = tmp(HEADS)
        bmax1 = tmp(1)
        diag8 = tmp(HEADS)
        attin = tmp(2 * RELS)
        jmask = tmp(FT)
        jp = tmp(2)
        jpi = tmp(2).bitcast(I32)
        visits = tmp(1)
        rowf = tmp(CH)
        parts_i = tmp(CH).bitcast(I32)
        parts = tmp(CH)
        part_col = tmp(CH)
        over = tmp(CH)

        CT = R1[:, :].rearrange("p (r k n) -> p r k n", r=2, k=NT)
        A16 = r2.bitcast(F16).rearrange("p (q k n) -> p q k n", q=2, k=NT)
        GX = r2[:, 0:NT * D * RELS].bitcast(F16).rearrange("p (r q k f) -> p r q k f", r=RELS, q=2, k=NT)
        XR = r2[:, 0:NT * D].rearrange("p (k f) -> p k f", k=NT)
        YT = r3.bitcast(F16).rearrange("p (r q f n) -> p r q f n", r=RELS, q=2, f=FT)
        XT16 = XX[:, NT * D:].bitcast(F16).rearrange("p (q f n) -> p q f n", q=2, f=FT)
        W16 = w_b.bitcast(F16).rearrange("p (s q f n) -> p s q f n", s=3, q=2, f=FT)

        def whole(region, at):
            return region[:, at:at + FT * D].rearrange("p (f n) -> p f n", f=FT)

        w_early = whole(r2, 2 * NT * D)
        HALVED = [(w_early, 0), (w_early, 1), (w_early, 2)] * 2 + [
            (whole(r2, NT * D), 0), (whole(r2, NT * D + FT * D), 1), (whole(r3, 4 * NN), 2),
            (whole(r3, 8 * NN - FT * D), 0)]
        trow = r2[0:1, NT * D * RELS:NT * D * RELS + NN]
        LNT = r2[:, NT * D * RELS + NN:NT * D * RELS + NN + 2 * D].rearrange("p (s f) -> p s f", s=2)
        ADJ = [adjin[:, 0], adjin[:, 1]] + [r1.bitcast(F32)[:, o:o + 2 * NN].rearrange("p (m r) -> p m r", m=2)
                                            for o in (NT * NN // 4, 3 * NT * NN // 4)]
        SUP = r3[:, 0:NT * D].bitcast(F16).rearrange("p (q k f) -> p q k f", q=2, k=NT)
        LNT0 = W[:, 2, 0:2, :]
        bns = stat[:, 0:6]
        mv = stat[:, 6:8]
        rstd = stat[:, 8:9]
        std = stat[:, 9:10]
        eps = stat[:, 10:11]
        def halves(region, slot, n):
            return region[0:n, slot * HEADS * NN // 2:(slot + 1) * HEADS * NN // 2].bitcast(F16).rearrange(
                "p (h n) -> p h n", h=HEADS)

        QHH = halves(r2, 0, P)
        QL = halves(r2, 1, DK + 1)
        KHL = halves(r3, 0, P)
        KH = halves(r3, 1, DK + 1)
        r1f = R1[:, :].bitcast(F32)
        VA = r1f[:, NT * NN // 2:NT * NN // 2 + NT * HEADS * (DK + 1)].rearrange(
            "p (k h e) -> p k h e", k=NT, h=HEADS)
        o1 = NT * NN // 2 + NT * HEADS * (DK + 1)
        mx = r1f[:, o1:o1 + NT * HEADS].rearrange("p (k h) -> p k h", k=NT)
        mxk = r1f[:, o1 + 80:o1 + 160]
        mxT = r1f[:, o1 + 160:o1 + 224].bitcast(F16)
        o2 = HEADS * NN
        nmask = r2[:, o2:o2 + NN].bitcast(BF16).rearrange("p (s n) -> p s n", s=2)
        junk = r2[:, o2 + NN:o2 + 2 * NN]
        yT = XT
        HB = 2 * ROWB
        ER = r1f[:, 0:2 * HB].rearrange("p (s n) -> p s n", s=2)
        BR = r1f[:, 2 * HB:6 * HB].rearrange("p (s n) -> p s n", s=4)
        den = r2[DK:DK + 1, o2:o2 + 2 * HB].rearrange("p (s n) -> p s n", s=2)
        denp = r1f[:, 7 * HB:7 * HB + HB // P]
        rden = r1f[:, 6 * HB:7 * HB]

        PS = ctx.enter_context(nc.psum_tensor("PS", [P, 8, 512], F32))

        def mm_out(b, n, m=P):
            return PS[0:m, b, 0:n]

        edges_in = sem("edges_in")
        const = sem("const")
        vs = sem("vs")
        ext_t = sem("ext_t")
        bexp = sem("bexp")
        tab_out = sem("tab_out")
        tab_in = sem("tab_in")
        ready = sem("ready")
        hot_made = sem("hot_made")
        hot_used = sem("hot_used")
        staged = [sem(f"staged{j}") for j in range(4)]
        stored = [sem(f"stored{j}") for j in range(4)]
        basis_in = [sem(f"basis_in{h}") for h in range(2)]
        w_done = sem("w_done")
        w_copied = sem("w_copied")
        w_stored = sem("w_stored")
        adj_in = [sem(f"adj_in{h}") for h in range(4)]
        sup_done = sem("sup_done")
        suph_made = sem("suph_made")
        sup_made = sem("sup_made")
        asum_made = sem("asum_made")
        a0h_made = sem("a0h_made")
        ct_made = sem("ct_made")
        a0_made = sem("a0_made")
        wgt_in = sem("wgt_in")
        late_in = [sem(f"late_in{i}") for i in range(4)]
        x_in = [sem(f"x_in{i}") for i in range(4)]
        agg_done = sem("agg_done")
        agg_free = sem("agg_free")
        z_done = sem("z_done")
        x_made = sem("x_made")
        bias_in = sem("bias_in")
        xt_done = sem("xt_done")
        xt_made = sem("xt_made")
        xth_made = sem("xth_made")
        yth_made = sem("yth_made")
        w16h_made = sem("w16h_made")
        w16_made = sem("w16_made")
        gate_done = sem("gate_done")
        gate_made = sem("gate_made")
        hi_made = sem("hi_made")
        lo_made = sem("lo_made")
        x1_out = sem("x1_out")
        x1_in = sem("x1_in")
        s2 = sem("s2")
        deg_done = sem("deg_done")
        q_done = sem("q_done")
        qkh_made = sem("qkh_made")
        qkl_made = sem("qkl_made")
        qk_copied = sem("qk_copied")
        v_done = sem("v_done")
        v_made = sem("v_made")
        mt_done = sem("mt_done")
        s_done = sem("s_done")
        s_used = sem("s_used")
        mxt_done = sem("mxt_done")
        mx_made = sem("mx_made")
        mxd = sem("mxd")
        mrow_in = sem("mrow_in")
        st_done = sem("st_done")
        e_made = sem("e_made")
        p_made = sem("p_made")
        bias_rd = [sem(f"bias_rd{i}") for i in range(4)]
        var_made = sem("var_made")
        std_made = sem("std_made")
        deg_copied = sem("deg_copied")
        dis_made = sem("dis_made")
        pool_made = sem("pool_made")
        ownb_made = sem("ownb_made")
        owna_made = sem("owna_made")
        a_built = sem("a_built")
        csum_made = sem("csum_made")
        x_pad = sem("x_pad")
        ps_zero = sem("ps_zero")
        t_made = sem("t_made")
        mxk_made = sem("mxk_made")
        pv_done = sem("pv_done")
        y_made = sem("y_made")
        den_in = sem("den_in")
        den_made = sem("den_made")
        rden_made = sem("rden_made")
        rden_out = sem("rden_out")
        den_out = [sem(f"den_out{i}") for i in range(2)]
        rden_in = [sem(f"rden_in{i}") for i in range(2)]
        yn_made = sem("yn_made")
        out_sem = sem("out_sem")

        block = ctx.enter_context(nc.Block())

        def within(v, least, most):
            return nc.s_assert_within(v, least, most,
                                      skip_runtime_bounds_check_because="made on the chip from chunk numbers")

        def tile_ranges(eng, t4):
            ap = tab[:, bass.ds(t4 * 4, 4)]
            _, vals = nc.values_load_multi_w_load_instructions(ap, engines=(eng.engine,), min_val=0,
                                                                max_val=2 ** 31 - 1)
            ranges = []
            for p in vals:
                first = within((p >> 8) & 255, 0, CH - 2)
                end = within(first + (p & 255), 2, CH)
                ranges.append((first, end, eng.snap(p >> 16)))
            return ranges

        def flat(ap):
            return ap.rearrange("p a b -> p (a b)")

        RELS_OF = [1, 2, 2, 1]
        GROUPS = [0] + [FT * r for r in RELS_OF[1:]]
        AGG0 = [NROWB * sum(GROUPS[:s]) for s in range(5)]
        THREE = [(0, 0), (1, 0), (0, 1)]
        PARTS0 = [NT * sum(RELS_OF[1:s]) for s in range(4)]
        NORMS = {0: 0, 2: 1, 3: 2, 4: 3}

        @block.sync
        def _(sp):
            sp.dma_start(dst_i[0:EC, :], a["dst_t"]).then_inc(edges_in, 16)
            sp.dma_start(dcm_i[0:HALF, :, :], a["dst_c"].rearrange("(g c) e -> c g e", g=2)).then_inc(edges_in, 16)
            sp.dma_start(src_i[0:EC, :], a["src_t"]).then_inc(edges_in, 16)
            sp.dma_start(typ_i[0:EC, :], a["type_t"]).then_inc(edges_in, 16)
            sp.dma_start(wgt[0:EC, :], a["weight_t"]).then_inc(edges_in, 16)
            sp.dma_start(attr[0:EC, :, :], a["attr_t"]).then_inc(edges_in, 16)
            for i in range(2):
                sp.dma_start(attin[0:BJ, RELS * i:RELS * (i + 1)], a[f"att{i + 1}_r"]).then_inc(edges_in, 16)
                sp.dma_start(gw[:, i, :, :], a[f"gate_w{i + 1}_t"].rearrange("p (t r) -> p t r", r=RELS)).then_inc(
                    edges_in, 16)
            sp.dma_start(qkb[:, 0, :], a["bq_t"]).then_inc(edges_in, 16)
            sp.dma_start(qkb[:, 1, :], a["bk_t"]).then_inc(edges_in, 16)
            sp.wait_ge(tab_out, 1)
            sp.dma_start(tab_d[0, :].rearrange("(t k) -> t k", k=1), tabi[0:TT, 0:1]).then_inc(tab_out, 16)
            sp.wait_ge(tab_out, 17)
            sp.dma_start(tab, tab_d).then_inc(tab_in, 16)

            def load_basis(layer, step, h):
                src = a[f"basis{layer + 1}"].rearrange("b (j t) n -> (b j) t n", j=FT)
                sp.dma_start(basis[0:BJ, h, :, :], src[:, bass.ds(step * 4, 4), :]).then_inc(basis_in[h], 16)

            def group(layer, t4, n4, prefetch):
                for j in range(4):
                    sp.wait_ge(staged[j], t4 + 2)
                    sp.dma_start(bias_d[bass.ds(t4 * (4 * MB) + j * MB, MB), :], stage[0:MB, j, :]).then_inc(
                        stored[j], 16)
                    sp.dma_start(adj_d[bass.ds(t4 * (4 * CW * MA) + j * CW * MA, CW * MA), :],
                                 stage[MB:MH, j, :]).then_inc(stored[j], 16)
                    if prefetch and j % 2:
                        sp.wait_ge(w_done, t4 * 2 + (j // 2 + 1))
                        load_basis(layer, n4 * 2 + (2 + j // 2), j // 2)
                sp.wait_ge(w_copied, t4 * 2 + 3)
                for c in range(4):
                    dst = w_d[layer].rearrange("q (s c) n -> q c s n", c=4)
                    sp.dma_start(dst[:, c, bass.ds(n4 * 2, 2), :], wst[32 * c:32 * c + RELS * FT, :, :]).then_inc(
                        w_stored, 16)

            def matrices_in(k, first, slot):
                sp.dma_start(ADJ[slot], adj_d.rearrange("(n m) r -> n m r", m=MA)[
                    bass.ds(k * P, P), first:first + 2, :]).then_inc(adj_in[slot], 16)

            for layer in range(2):
                if layer:
                    sp.wait_ge(w_done, 32)
                for h in range(2):
                    load_basis(layer, h, h)
                if layer == 0:
                    with sp.Fori(0, 15) as t4:
                        group(0, t4, t4, True)
                    group(0, 15, 15, False)
                else:
                    for j in range(4):
                        sp.wait_ge(stored[j], 32 * 17)
                    with sp.Fori(0, NT // 2) as k:
                        for q in range(3):
                            group(1, k * 3 + (16 + q), k * 3 + q, True)
                        sp.wait_ge(ct_made, k * RELS + 1)
                        matrices_in(k, 0, 0)
                    group(1, 31, 15, False)
            sp.wait_ge(a_built, 1)
            for k in range(0, NT - 1, 3):
                sp.dma_start(X[:, k:k + 3, :], a["x"][k * P:(k + 3) * P, :].rearrange("(k p) f -> p k f", p=P)).then_inc(
                    x_in[k // 3], 16)
            sp.wait_ge(x_pad, 1)
            sp.dma_start(X[0:LAST, NT - 1, :], a["x"][(NT - 1) * P:NODES, :]).then_inc(x_in[3], 16)

            def load_whole(dst, src, loaded=wgt_in):
                sp.dma_start(dst, src.rearrange("(t p) n -> p t n", p=P)).then_inc(loaded, 16)

            def load_b(name):
                sp.dma_start(brow[:, :], a[name].rearrange("(u n) -> u n", u=1)).then_inc(bias_in, 16)

            load_whole(W[:, 0, :, :], a["W0"])
            load_b("b0")
            for j in range(4):
                sp.wait_ge(stored[j], 32 * 33)
            sp.wait_ge(w_stored, 64 * 32 + 16)
            for n in range(NT + NT // 2):
                if n == 0:
                    sp.wait_ge(ct_made, NT + 1)
                elif n >= 4:
                    sp.wait_ge(a0_made, n - 3 if n < NT else min(n - 1, NT))
                    if n - 2 >= NT:
                        sp.wait_ge(ct_made, NT + 2 * (n - 1 - NT) + 1)
                if n < NT:
                    matrices_in(n, 2, n % 4)
                else:
                    matrices_in(n - NT // 2, 0, n % 2)
            for i in range(2):
                sp.wait_ge(z_done, NT * (i + 1))
                sp.wait_ge(x_made, NT * (i + 1))
                if i == 0:
                    sp.dma_start(x1_d, X[:, :, :].rearrange("p k f -> p (k f)")).then_inc(x1_out, 16)
                for r in range(RELS):
                    if 3 * i + r:
                        sp.wait_ge(w16_made, 3 * i + r)
                    sp.dma_start(w_early, w_d[i][FT * r:FT * (r + 1), :, :].rearrange("t p n -> p t n")).then_inc(
                        wgt_in, 16)
                sp.wait_ge(w16_made, 3 * i + 2)
                load_whole(w_early, a[f"root{i + 1}"])
                load_b(f"bias{i + 1}")
            sp.wait_ge(agg_done, AGG0[3])
            sp.wait_ge(x1_out, 16)
            sp.dma_start(XR.rearrange("p k f -> p (k f)"), x1_d).then_inc(x1_in, 16)
            sp.wait_ge(z_done, NT * 3)
            for n, name in enumerate(("W2", "Wq", "Wk", "Wv")):
                load_whole(HALVED[6 + n][0], a[name], late_in[n])
            load_b("b2")
            sp.wait_ge(z_done, NT * 4)
            load_b("bv")
            sp.wait_ge(w16_made, len(HALVED))
            for o_ in range(FT):
                hs = slice(2 * o_, 2 * o_ + 2)
                sp.wait_ge(qkh_made, 6 * o_ + 6)
                sp.dma_start(QHH[DK:P, hs, :], QHH[0:DK, hs, :]).then_inc(qk_copied, 16)
                sp.dma_start(KH[0:DK, hs, :], KHL[0:DK, hs, :]).then_inc(qk_copied, 16)
            sp.wait_ge(mx_made, 1)
            sp.dma_start(max_d, mxT[0:NT * HEADS, :]).then_inc(mxd, 16)
            sp.wait_ge(mxd, 16)
            sp.dma_start(QL[DK:DK + 1, :, :].rearrange("p h (k n) -> p h k n", n=P),
                         max_d.rearrange("(u k h) n -> u h k n", u=1, h=HEADS)).then_inc(mrow_in, 16)
            load_whole(W[:, 1, :, :], a["Wo"])
            sp.wait_ge(v_made, 2 * NT)
            load_b("bo")
            def store_den(rb, h):
                g = rb * HEADS + h
                sp.wait_ge(y_made, g * 2 + 6)
                sp.dma_start(den_d[h:h + 1, bass.ds(rb * HB, HB)], den[:, h % 2, :]).then_inc(den_out[h % 2], 16)

            def on_partitions(m, rb, h):
                return m[h:h + 1, bass.ds(rb * HB, HB)].rearrange("u (p n) -> (u p) n", p=P)

            def load_den(rb, h):
                sp.wait_ge(den_out[h % 2], rb * (8 * HEADS) + 16 * (h // 2 + 2))
                sp.dma_start(denp, on_partitions(den_d, rb, h)).then_inc(den_in, 16)

            def store_rden(rb, h):
                sp.wait_ge(rden_made, rb * HEADS + (h + 1))
                sp.dma_start(on_partitions(rden_d, rb, h), denp).then_inc(rden_out, 16)

            def spread_rden(rb, h):
                sp.wait_ge(rden_out, rb * (16 * HEADS) + 16 * (h + 1))
                sp.wait_ge(yn_made, rb * HEADS + (h + 1))
                sp.dma_start(rden[DK * (h % 2):DK * (h % 2 + 1), :],
                             rden_d[h:h + 1, bass.ds(rb * HB, HB)].broadcast_to([DK, HB])).then_inc(rden_in[h % 2], 16)

            sp.wait_ge(mxk_made, 1)
            with sp.Fori(0, 2) as rb:
                for n in range(HEADS * NT):
                    h, j = divmod(n, NT)
                    sp.wait_ge(pv_done, rb * (HEADS * NT) + (n + 1))
                    sp.dma_start(BR[:, n % 4, :], bias_d.rearrange("(n h) r -> n h r", h=HEADS)[
                        j * P:(j + 1) * P, h, bass.ds(rb * HB, HB)]).then_inc(bias_rd[n % 4], 16)
                    if h >= 1 and j in (4, 6, 9):
                        {4: store_den, 6: load_den, 9: store_rden}[j](rb, h - 1)
                    if h >= 2 and j == 1:
                        spread_rden(rb, h - 2)
                spread_rden(rb, HEADS - 2)
                for step_of in (store_den, load_den, store_rden, spread_rden):
                    step_of(rb, HEADS - 1)
            for i in range(NT):
                n = P if i < NT - 1 else LAST
                sp.wait_ge(x_made, 4 * NT + i + 1)
                sp.dma_start(out[i * P:i * P + n, :], X[0:n, i, :]).then_inc(out_sem, 16)
            sp.wait_ge(out_sem, 16 * NT)

        @block.gpsimd
        def _(pool):
            pool.iota(iota16, [[1, NN]], base=0, channel_multiplier=0,
                      allow_small_or_imprecise_dtypes=True).then_inc(const, 1)
            pool.iota(pidx[:, :], [[0, 1]], base=0, channel_multiplier=1,
                      allow_small_or_imprecise_dtypes=True).then_inc(const, 1)
            pool.iota(jpi[:, 0:1], [[0, 1]], base=0, channel_multiplier=1).then_inc(const, 1)
            pool.memset(ones[:, :], 1.0).then_inc(const, 1)
            pool.memset(eps, EPS).then_inc(const, 1)
            pool.memset(one16[:, :], 1.0).then_inc(const, 1)
            pool.memset(ident[:, :], 0.0).then_inc(const, 1)
            pool.memset(ident16[:, :], 0.0).then_inc(const, 1)
            pool.memset(upper[:, :], 1.0).then_inc(const, 1)
            pool.wait_ge(const, 9)
            for m in (ident, ident16):
                pool.affine_select(out=m[:, :], in_=m[:, :], compare_op=ALU.not_equal, fill=1.0,
                                   base=0, pattern=[[-1, P]], channel_multiplier=1).then_inc(const, 1)
            pool.affine_select(out=upper, in_=upper, compare_op=ALU.is_ge, fill=0.0,
                               base=0, pattern=[[1, TT]], channel_multiplier=-1).then_inc(const, 1)
            pool.wait_ge(ready, 3)
            pool.tensor_tensor(ownH[0:EC, :, MB:MH].rearrange("p c (w m) -> p c w m", m=MA),
                               eq[0:EC, :, :].rearrange("p c (w u) -> p c w u", u=1).broadcast_to([EC, CH, CW, MA]),
                               valA[0:EC, :, :].rearrange("p c (u m) -> p c u m", u=1).broadcast_to([EC, CH, CW, MA]),
                               ALU.mult).then_inc(owna_made, 1)
            pool.wait_ge(a_built, 1)
            pool.memset(X[:, NT - 1, :], 0.0).then_inc(x_pad, 1)

            for n, (src, slot) in enumerate(HALVED):
                if n < 6:
                    pool.wait_ge(wgt_in, 16 * (n + 2))
                else:
                    pool.wait_ge(late_in[n - 6], 16)
                if n == len(HALVED) - 1:
                    pool.wait_ge(z_done, 4 * NT)
                pool.tensor_copy(W16[:, slot, 0, :, :], src).then_inc(w16h_made, 1)
                pool.wait_ge(w16h_made, n + 1)
                pool.tensor_tensor(W16[:, slot, 1, :, :], src, W16[:, slot, 0, :, :], ALU.subtract).then_inc(
                    w16_made, 1)
            pool.wait_ge(w16_made, len(HALVED))
            pool.wait_ge(z_done, 4 * NT)
            pool.memset(KH[DK:DK + 1, :, :], MSCALE).then_inc(pool_made, 1)
            pool.wait_ge(pool_made, 1)
            pool.memset(VA[:, :, :, DK:DK + 1], 1.0).then_inc(pool_made, 1)
            pool.sem_inc(yn_made, 2)
            with pool.Fori(0, 2) as rb:
                for h in range(HEADS):
                    rows, cols = slice(DK * (h % 2), DK * (h % 2 + 1)), bass.ds(rb * HB, HB)
                    d, y = rden[rows, :], yT[rows, h // 2, cols]
                    pool.wait_ge(rden_in[h % 2], rb * (8 * HEADS) + 16 * (h // 2 + 1))
                    pool.wait_ge(y_made, rb * (2 * HEADS) + (2 * h + 6))
                    pool.tensor_tensor(y, y, d, ALU.mult).then_inc(yn_made, 1)

        CONST = 12
        EDGE_LOADS = 12

        @block.vector
        def _(dve):
            V = nc.vector
            chain = [0]

            def step(ins):
                chain[0] += 1
                ins.then_inc(vs, 1)
                dve.wait_ge(vs, chain[0])

            V.memset(PS[:, 6:8, :], 0.0).then_inc(ps_zero, 1)
            dve.sem_inc(hot_made, CH)
            dve.wait_ge(const, CONST)
            dve.wait_ge(edges_in, 16 * EDGE_LOADS)
            step(V.tensor_copy(dcm[0:HALF, :, :], dcm_i[0:HALF, :, :]))
            V.tensor_reduce(ext[0:HALF, 0:2], dcm[0:HALF, :, :], AX.X, ALU.min)
            step(V.tensor_reduce(ext[0:HALF, 2:4], dcm[0:HALF, :, :], AX.X, ALU.max))
            for q in range(4):
                ins = V.tensor_scalar(diag4[0:HALF, q, :], ident[0:HALF, 0:HALF], ext[0:HALF, q:q + 1], None, ALU.mult)
            ins.then_inc(ready, 1)
            step(V.tensor_reduce(bmax[0:EC, :], attr[0:EC, :, :].rearrange("p c h -> p h c"), AX.X, ALU.max))
            step(V.tensor_copy(rowf[0:EC, :], src_i[0:EC, :]))
            step(V.tensor_scalar(flat(base[0:EC, :, :]), iota16[0:EC, 0:TT], float(NN), None, ALU.mult))
            step(V.tensor_copy(part_col[0:EC, :], dst_i[0:EC, :]))
            step(V.tensor_scalar(parts_i[0:EC, :], part_col[0:EC, :], 1.0 / CW, None, ALU.mult))
            step(V.tensor_copy(parts[0:EC, :], parts_i[0:EC, :]))
            step(V.scalar_tensor_tensor(part_col[0:EC, :], parts[0:EC, :], -float(CW), part_col[0:EC, :], ALU.mult,
                                        ALU.add))
            for test, by in ((ALU.is_lt, -1.0), (ALU.is_ge, 1.0)):
                edge = 0.0 if by < 0 else float(CW)
                step(V.tensor_scalar(over[0:EC, :], part_col[0:EC, :], edge, by, test, ALU.mult))
                step(V.tensor_tensor(parts[0:EC, :], parts[0:EC, :], over[0:EC, :], ALU.add))
                step(V.scalar_tensor_tensor(part_col[0:EC, :], over[0:EC, :], -float(CW), part_col[0:EC, :], ALU.mult,
                                            ALU.add))
            step(V.scalar_tensor_tensor(key[0:EC, :], parts[0:EC, :], float(NN), rowf[0:EC, :], ALU.mult, ALU.add))
            step(V.tensor_tensor(eq[0:EC, :, :],
                                 part_col[0:EC, :].rearrange("p (c u) -> p c u", u=1).broadcast_to([EC, CH, CW]),
                                 iota16[0:EC, 0:CW].rearrange("p (u w) -> p u w", u=1).broadcast_to([EC, CH, CW]),
                                 ALU.is_equal))
            V.tensor_copy(rowf[0:EC, 0:1], rowf[0:EC, 0:1]).then_inc(ready, 1)
            step(V.tensor_copy(gw16[:, 0, :, :, :], gw[:, :, :, :]))
            V.tensor_tensor(gw16[:, 1, :, :, :], gw[:, :, :, :], gw16[:, 0, :, :, :], ALU.subtract)
            V.tensor_scalar(valA[0:EC, :, 0], typ_i[0:EC, :], 0, None, ALU.is_equal)
            V.tensor_scalar(valA[0:EC, :, 1], typ_i[0:EC, :], 0, None, ALU.not_equal)
            step(V.tensor_copy(valA[0:EC, :, 2], wgt[0:EC, :]))
            V.tensor_tensor(valA[0:EC, :, 3], wgt[0:EC, :], valA[0:EC, :, 2], ALU.subtract)
            step(V.tensor_scalar(jpi[:, 1:2], jpi[:, 0:1], FT - 1, None, ALU.bitwise_and))
            step(V.tensor_copy(jp[:, 0:1], jpi[:, 1:2]))
            step(V.tensor_scalar(jmask, iota16[:, 0:FT], jp[:, 0:1], None, ALU.is_equal))
            for i in range(2 * RELS):
                ins = V.tensor_scalar(attbd[0:BJ, i // RELS, i % RELS, :], jmask[0:BJ, :], attin[0:BJ, i:i + 1],
                                      None, ALU.mult)
            ins.then_inc(ready, 1)
            dve.wait_ge(ext_t, 2)
            step(V.tensor_reduce(bmax1[0:HEADS, :], mm_out(1, EC, HEADS), AX.X, ALU.max))
            V.tensor_scalar(diag8[0:HEADS, :], ident[0:HEADS, 0:HEADS], bmax1[0:HEADS, :], None, ALU.mult).then_inc(
                ready, 1)
            step(V.tensor_copy(crow[0:TT, :], mm_out(0, 4 * HALF, TT)))
            V.tensor_scalar(bound[0:TT, 0:1], pidx[0:TT, :], float(CW), None, ALU.mult)
            step(V.tensor_scalar(bound[0:TT, 1:2], pidx[0:TT, :], float(CW), float(CW - 1), ALU.mult, ALU.add))
            step(V.tensor_scalar(inside[0:TT, :], crow[0:TT, 0:CH], bound[0:TT, 1:2], None, ALU.is_le))
            step(V.scalar_tensor_tensor(cond[0:TT, :], crow[0:TT, CH:2 * CH], bound[0:TT, 0:1], inside[0:TT, :],
                                        ALU.is_ge, ALU.mult))
            step(V.tensor_scalar(ramp[0:TT, :], iota16[0:TT, 0:CH], -1.0, float(CH), ALU.mult, ALU.add))
            step(V.tensor_tensor(val[0:TT, :], cond[0:TT, :], ramp[0:TT, :], ALU.mult))
            step(V.tensor_reduce(lohi[0:TT, 0:1], val[0:TT, :], AX.X, ALU.max))
            step(V.tensor_scalar(lohi[0:TT, 0:1], lohi[0:TT, 0:1], -1.0, float(CH), ALU.mult, ALU.add))
            step(V.tensor_scalar(lohi[0:TT, 0:1], lohi[0:TT, 0:1], float(CH - 2), None, ALU.min))
            step(V.tensor_scalar(ramp[0:TT, :], iota16[0:TT, 0:CH], 1.0, None, ALU.add))
            step(V.tensor_tensor(val[0:TT, :], cond[0:TT, :], ramp[0:TT, :], ALU.mult))
            step(V.tensor_reduce(lohi[0:TT, 1:2], val[0:TT, :], AX.X, ALU.max))
            step(V.scalar_tensor_tensor(lohi[0:TT, 1:2], lohi[0:TT, 0:1], 2.0, lohi[0:TT, 1:2], ALU.add, ALU.max))
            V.tensor_tensor(visits[0:TT, :], lohi[0:TT, 1:2], lohi[0:TT, 0:1], ALU.subtract).then_inc(ready, 1)
            dve.wait_ge(ext_t, 4)
            step(V.tensor_tensor(bound[0:TT, 0:1], PS[0:TT, 3, 0:1], lohi[0:TT, 1:2], ALU.subtract))
            step(V.tensor_scalar(bound[0:TT, 0:1], bound[0:TT, 0:1], float(CH), None, ALU.add))
            V.tensor_copy(tabi[0:TT, 0:1], bound[0:TT, 0:1])
            V.tensor_copy(tabi[0:TT, 1:2], lohi[0:TT, 0:1])
            step(V.tensor_copy(tabi[0:TT, 2:3], visits[0:TT, :]))
            for k in range(2):
                step(V.tensor_scalar(tabi[0:TT, 0:1], tabi[0:TT, 0:1], 8, None, ALU.logical_shift_left))
                step(V.tensor_tensor(tabi[0:TT, 0:1], tabi[0:TT, 0:1], tabi[0:TT, k + 1:k + 2], ALU.bitwise_or))
            V.tensor_copy(rowf[0:TT, 0:1], visits[0:TT, :]).then_inc(tab_out, 1)
            bm = PS[0:EC, 2, 0:HEADS]
            for h in range(HEADS):
                ins = V.tensor_scalar(attr[0:EC, :, h], attr[0:EC, :, h], PS[0:EC, 2, h:h + 1], None, ALU.subtract)
            ins.then_inc(ready, 1)
            dve.wait_ge(bexp, 1)
            step(V.tensor_scalar(attr[0:EC, :, :], attr[0:EC, :, :], 32768.0, None, ALU.mult))
            step(V.tensor_copy(valBh[0:EC, :, :], attr[0:EC, :, :]))
            step(V.tensor_tensor(valBl[0:EC, :, :], attr[0:EC, :, :], valBh[0:EC, :, :], ALU.subtract))
            for dst, vals in ((ownH, valBh), (ownL, valBl)):
                V.tensor_tensor(dst[0:EC, :, 0:MB].rearrange("p c (w m) -> p c w m", m=HEADS),
                                eq[0:EC, :, :].rearrange("p c (w u) -> p c w u", u=1).broadcast_to(
                                    [EC, CH, CW, HEADS]),
                                vals[0:EC, :, :].rearrange("p c (u m) -> p c u m", u=1).broadcast_to(
                                    [EC, CH, CW, HEADS]), ALU.mult).then_inc(ownb_made, 1)
            dve.wait_ge(owna_made, 1)
            dve.wait_ge(ownb_made, 2)
            dve.wait_ge(tab_in, 16)

            def make(rng, t4, j):
                lo, hi, off = rng
                with dve.Fori(lo, hi) as c:
                    v = c + off
                    dve.wait_ge(hot_used, v + 1)
                    V.tensor_scalar(flat(hot[0:EC, bass.ds(v & (HOTS - 1), 1), :]), iota16[0:EC, :],
                                    base[0:EC, bass.ds(t4, 1), j], key[0:EC, bass.ds(c, 1)], ALU.add,
                                    ALU.is_equal).then_inc(hot_made, 1)

            with dve.Fori(0, TT // 4) as t4:
                rngs = tile_ranges(dve, t4)
                for j in range(4):
                    make(rngs[j], t4, j)
            dve.wait_ge(a_built, 1)
            for k in range(NT + 3):
                if k < NT:
                    dve.wait_ge(adj_in[k % 4], 16 * (k // 4 + 1 + (NT // 2 if k % 4 == 0 else 0)))
                    V.tensor_tensor(ADJ[k % 4][:, 0, :], ADJ[k % 4][:, 0, :], ADJ[k % 4][:, 1, :],
                                    ALU.add).then_inc(asum_made, 1)
                if 1 <= k <= NT:
                    dve.wait_ge(a0h_made, k)
                    V.tensor_tensor(A16[:, 1, k - 1, :], ADJ[(k - 1) % 4][:, 0, :], A16[:, 0, k - 1, :],
                                    ALU.subtract).then_inc(a0_made, 1)
                if k >= 3:
                    dve.wait_ge(suph_made, k - 2)
                    V.tensor_tensor(SUP[:, 1, k - 3, :], mm_out((k - 1) % 4, D), SUP[:, 0, k - 3, :],
                                    ALU.subtract).then_inc(sup_made, 1)

            def norm(s, i):
                dve.wait_ge(z_done, s * NT + i + 1)
                z = mm_out(4 + i % 2, D)
                r = (LNT if s else LNT0)[:, i % 2, :]
                if s == 3:
                    step(V.scalar_tensor_tensor(r, z, dis[:, i:i + 1], X[:, i, :], ALU.mult, ALU.add))
                elif s == 2:
                    step(V.tensor_tensor(r, z, XR[:, i, :], ALU.add))
                else:
                    step(V.tensor_tensor(r, z, X[:, i, :], ALU.add))
                step(V.bn_stats(bns, r))
                V.bn_aggr(mv, bns).then_inc(var_made, 1)
                dve.wait_ge(std_made, NORMS[s] * NT + i + 1)
                step(V.reciprocal(rstd, std))
                V.tensor_scalar(X[:, i, :], r, mv[:, 0:1], rstd, ALU.subtract, ALU.mult).then_inc(x_made, 1)
                dve.wait_ge(x_made, s * NT + i + 1)

            def low_parts(done, rels, scale):
                for r in range(rels):
                    for k in range(NT):
                        done += 1
                        dve.wait_ge(hi_made, done)
                        V.scalar_tensor_tensor(GX[:, r, 1, k, :], X[:, k, :], scale(k, r), GX[:, r, 0, k, :],
                                               ALU.mult, ALU.subtract).then_inc(lo_made, 1)

            def turned_low(n, i):
                dve.wait_ge(xth_made, n + i + 1)
                V.tensor_tensor(XT16[:, 1, :, i * P:(i + 1) * P],
                                PS[:, 6 + i % 2, :].rearrange("p (a b) -> p a b", a=FT),
                                XT16[:, 0, :, i * P:(i + 1) * P], ALU.subtract).then_inc(xt_made, 1)

            def normed_and_turned_low(s, n):
                for i in range(NT + 2):
                    if i < NT:
                        norm(s, i)
                    if i >= 2:
                        turned_low(n, i - 2)

            def aggregated_low(s):
                with dve.Fori(0, NROWB) as rb:
                    for g in range(GROUPS[s]):
                        dve.wait_ge(yth_made, rb * GROUPS[s] + (AGG0[s] + g + 1))
                        V.tensor_tensor(YT[:, g // FT, 1, g % FT, bass.ds(rb * ROWB, ROWB)], PS[:, g % 4, 0:ROWB],
                                        YT[:, g // FT, 0, g % FT, bass.ds(rb * ROWB, ROWB)],
                                        ALU.subtract).then_inc(agg_free, 1)

            normed_and_turned_low(0, 0)
            for layer in range(2):
                dve.wait_ge(gate_made, layer + 1)
                low_parts(layer * NT * RELS, RELS, lambda k, r: gate[:, k, r:r + 1])
                aggregated_low(1 + layer)
                if layer == 0:
                    for i in range(NT):
                        turned_low(NT, i)
            dve.wait_ge(agg_done, AGG0[3])
            ct = R1[:, :]
            step(V.tensor_tensor(ct[:, 0:NT * NN], ct[:, 0:NT * NN], ct[:, NT * NN:], ALU.add))
            step(V.tensor_copy(ct[:, NT * NN:], ct[:, 0:NT * NN]))
            for k in range(NT):
                blk = CT[:, 1, k, k * P:(k + 1) * P]
                ins = V.tensor_tensor(blk, blk, ident16[:, :], ALU.add)
            ins.then_inc(csum_made, 1)
            dve.wait_ge(x1_in, 16)
            for i in range(NT):
                norm(2, i)
            dve.wait_ge(deg_done, 1)
            V.tensor_copy(degs[:, :], mm_out(0, NT)).then_inc(deg_copied, 1)
            dve.wait_ge(dis_made, 1)
            step(V.reciprocal(dis[:, :], dis[:, :]))
            step(V.tensor_copy(dis16[:, 0, :], dis[:, :]))
            V.tensor_tensor(dis16[:, 1, :], dis[:, :], dis16[:, 0, :], ALU.subtract).then_inc(s2, 1)
            low_parts(2 * NT * RELS, 1, lambda k, r: dis[:, k:k + 1])
            aggregated_low(3)
            normed_and_turned_low(3, 2 * NT)
            for g in range(2 * FT * 3):
                o_, which, p_ = g // 6, g // 3 % 2, g % 3
                lo, hi = PIECES[p_]
                dve.wait_ge(qkh_made, g + 1)
                for e in range(2):
                    h = 2 * o_ + e
                    high = (QHH, KHL)[which][0:DK, h, lo:hi]
                    low = KHL[DK:P, h, lo:hi] if which else QL[0:DK, h, lo:hi]
                    ins = V.scalar_tensor_tensor(low, PS[DK * e:DK * (e + 1), g % 4, 0:hi - lo],
                                                 qkb[:, which, h:h + 1], high, ALU.add, ALU.subtract)
                ins.then_inc(qkl_made, 1)
            for i in range(NT):
                dve.wait_ge(mt_done, i + 1)
                step(V.tensor_scalar(nmask[:, i % 2, :],
                                     PS[:, 6:8, :].rearrange("p a b -> p (a b)").bitcast(F16)[:, 0:NN],
                                     0.0, -BIG, ALU.is_equal, ALU.mult))
                for h in range(HEADS):
                    idx = i * HEADS + h
                    dve.wait_ge(s_done, idx + 1)
                    b0 = 3 * (idx % 2)
                    V.tensor_tensor_reduce(out=junk, in0=PS[:, b0:b0 + 3, :].rearrange("p a b -> p (a b)")[:, 0:NN],
                                           in1=nmask[:, i % 2, :], scale=1.0, scalar=-3e38, op0=ALU.add, op1=ALU.max,
                                           accum_out=mx[:, i, h:h + 1]).then_inc(s_used, 1)
                    dve.wait_ge(s_used, idx + 1)
            mxf = mx.rearrange("p a b -> p (a b)")
            V.scalar_tensor_tensor(mxk, mxf, -BIG / 10, mxf, ALU.is_gt, ALU.mult).then_inc(mxk_made, 1)
            dve.wait_ge(mxt_done, 1)
            V.tensor_scalar(mxT[0:NT * HEADS, :], mm_out(0, P, NT * HEADS), -1.0 / MSCALE, None, ALU.mult).then_inc(mx_made, 1)
            dve.sem_inc(p_made, 2)

            def reciprocals(rb, h):
                dve.wait_ge(den_in, rb * (16 * HEADS) + 16 * (h + 1))
                V.tensor_scalar(denp, denp, 1e-30, None, ALU.max).then_inc(den_made, 1)
                dve.wait_ge(den_made, rb * HEADS + (h + 1))
                V.reciprocal(denp, denp).then_inc(rden_made, 1)

            with dve.Fori(0, 2) as rb:
                for n in range(HEADS * NT):
                    u = rb * (HEADS * NT) + n
                    dve.wait_ge(e_made, u + 3)
                    dve.wait_ge(bias_rd[n % 4], rb * (16 * HEADS * NT // 4) + 16 * (n // 4 + 1))
                    V.scalar_tensor_tensor(BR[:, n % 4, :], ER[:, n % 2, :], BIG, BR[:, n % 4, :], ALU.min,
                                           ALU.mult).then_inc(p_made, 1)
                    if n >= NT and n % NT == 8:
                        reciprocals(rb, n // NT - 1)
                reciprocals(rb, HEADS - 1)
            for i in range(NT):
                norm(4, i)

        @block.scalar
        def _(act):
            S = nc.scalar
            act.wait_ge(ready, 6)
            S.activation(attr[0:EC, :, :], attr[0:EC, :, :], ACT.Exp).then_inc(bexp, 1)
            for j in range(4):
                act.sem_inc(stored[j], 32)
                act.sem_inc(staged[j], 1)
            act.sem_inc(w_copied, 1)
            act.sem_inc(w_stored, 16)
            act.sem_inc(ct_made, 1)
            act.sem_inc(t_made, 1)
            act.wait_ge(tab_in, 16)

            def group(t4):
                rngs = tile_ranges(act, t4)
                for j in range(4):
                    lo, hi, off = rngs[j]
                    act.wait_ge(hot_used, hi + off + HOTS)
                    act.wait_ge(stored[j], t4 * 32 + 32)
                    S.activation(stage[0:MH, j, :], PS[0:MH, 3 * (j % 2):3 * (j % 2) + 3, :].rearrange(
                        "p a b -> p (a b)")[:, 0:NN], ACT.Copy).then_inc(staged[j], 1)
                    if j % 2:
                        act.wait_ge(w_done, t4 * 2 + (j // 2 + 1))
                        act.wait_ge(w_stored, t4 * 64 + 16)
                        S.activation(wst[:, j // 2, :], PS[:, 6 + j // 2, :], ACT.Copy).then_inc(w_copied, 1)

            def counts(k, slot, n):
                act.wait_ge(adj_in[slot], n)
                for r in range(RELS):
                    S.activation(flat(CT[:, r, bass.ds(k, 1), :]), adjin[:, slot, r, :], ACT.Copy).then_inc(
                        ct_made, 1)

            with act.Fori(0, 16) as t4:
                group(t4)
            with act.Fori(0, NT // 2) as k:
                for q in range(3):
                    group(k * 3 + (16 + q))
                counts(k, 0, k * 16 + 16)
            group(31)
            act.wait_ge(a_built, 1)
            for j in range(4):
                act.wait_ge(stored[j], 32 * 33)

            def deviation(s, i):
                act.wait_ge(var_made, NORMS[s] * NT + i + 1)
                S.activation(std, mv[:, 1:2], ACT.Sqrt, bias=eps).then_inc(std_made, 1)

            def normed_and_turned(s, n):
                for i in range(NT + 1):
                    if i < NT:
                        deviation(s, i)
                    if i >= 1:
                        transposed(n, i - 1)
                    if s == 0 and i % 2 and i < NT:
                        m = NT + i // 2
                        counts(m - NT // 2, m % 2, 16 * ((m - NT) // 2 + 4 + (NT // 2 if m % 2 == 0 else 0)))

            def aggregated(s):
                with act.Fori(0, NROWB) as rb:
                    for g in range(GROUPS[s]):
                        act.wait_ge(agg_done, rb * GROUPS[s] + (AGG0[s] + g + 1))
                        S.activation(YT[:, g // FT, 0, g % FT, bass.ds(rb * ROWB, ROWB)], PS[:, g % 4, 0:ROWB],
                                     ACT.Copy).then_inc(yth_made, 1)
                    if s == 3:
                        act.wait_ge(deg_done, rb + 2)
                        S.activation(trow[:, bass.ds(rb * ROWB, ROWB)], PS[0:1, 4, 0:ROWB], ACT.Copy).then_inc(
                            t_made, 1)

            def transposed(n, i):
                act.wait_ge(xt_done, n + i + 1)
                S.activation(XT16[:, 0, :, i * P:(i + 1) * P],
                             PS[:, 6 + i % 2, :].rearrange("p (a b) -> p a b", a=FT), ACT.Copy).then_inc(xth_made, 1)

            def high_parts(rels, scale):
                for r in range(rels):
                    for k in range(NT):
                        S.activation(GX[:, r, 0, k, :], X[:, k, :], ACT.Copy, scale=scale(k, r)).then_inc(hi_made, 1)

            for i in range(NT + 2):
                if i < NT:
                    act.wait_ge(xt_done, i + 1)
                    S.activation(XT[:, :, i * P:(i + 1) * P],
                                 PS[:, 6 + i % 2, :].rearrange("p (a b) -> p a b", a=FT), ACT.Copy).then_inc(xt_made, 1)
                if i >= 2:
                    act.wait_ge(sup_done, i - 1)
                    S.activation(SUP[:, 0, i - 2, :], mm_out(i % 4, D), ACT.Copy).then_inc(suph_made, 1)
                if i < NT:
                    act.wait_ge(asum_made, i + 1)
                    S.activation(A16[:, 0, i, :], ADJ[i % 4][:, 0, :], ACT.Copy).then_inc(a0h_made, 1)
            normed_and_turned(0, NT)
            for layer in range(2):
                act.wait_ge(gate_done, NT * (layer + 1))
                S.activation(gate[:, :, :].rearrange("p a b -> p (a b)"), mm_out(0, NT * RELS), ACT.Sigmoid).then_inc(
                    gate_made, 1)
                act.wait_ge(gate_made, layer + 1)
                act.wait_ge(x_made, NT * (layer + 1))
                high_parts(RELS, lambda k, r: gate[:, k, r:r + 1])
                aggregated(1 + layer)
                if layer == 0:
                    act.wait_ge(x1_out, 16)
                    for i in range(NT + 2):
                        if i < NT:
                            act.wait_ge(z_done, NT + i + 1)
                            S.activation(X[:, i, :], mm_out(4 + i % 2, D), ACT.Relu).then_inc(x_made, 1)
                        if i >= 2:
                            transposed(2 * NT, i - 2)
            for i in range(NT):
                deviation(2, i)
            act.wait_ge(deg_copied, 1)
            S.activation(dis[:, :], degs[:, :], ACT.Sqrt).then_inc(dis_made, 1)
            act.wait_ge(s2, 1)
            act.wait_ge(x_made, 3 * NT)
            high_parts(1, lambda k, r: dis[:, k:k + 1])
            aggregated(3)
            normed_and_turned(3, 3 * NT)
            act.wait_ge(z_done, 4 * NT)
            for g in range(2 * FT * 3):
                o_, which, p_ = g // 6, g // 3 % 2, g % 3
                lo, hi = PIECES[p_]
                act.wait_ge(q_done, g + 1)
                for e in range(2):
                    h = 2 * o_ + e
                    ins = S.activation((QHH, KHL)[which][0:DK, h, lo:hi], PS[DK * e:DK * (e + 1), g % 4, 0:hi - lo],
                                       ACT.Identity, bias=qkb[:, which, h:h + 1])
                ins.then_inc(qkh_made, 1)
            for n in range(2 * NT):
                i, half = divmod(n, 2)
                act.wait_ge(v_done, n + 1)
                S.activation(VA[:, i, 4 * half:4 * half + 4, 0:DK],
                             PS[:, 7, 128:128 + D // 2].rearrange("p (h e) -> p h e", h=4), ACT.Copy).then_inc(
                                 v_made, 1)
            act.sem_inc(e_made, 2)
            act.sem_inc(y_made, 4)
            for i in range(2):
                act.sem_inc(den_out[i], 16)
            act.wait_ge(mxk_made, 1)

            def head_out(rb, h):
                g = rb * HEADS + h
                act.wait_ge(pv_done, g * NT + (NT + 4))
                b0 = 4 + 2 * (h % 2)
                S.activation(yT[DK * (h % 2):DK * (h % 2 + 1), h // 2, bass.ds(rb * HB, HB)].rearrange(
                    "p (a b) -> p a b", a=2), PS[0:DK, b0:b0 + 2, 0:ROWB], ACT.Copy).then_inc(y_made, 1)
                act.wait_ge(den_out[h % 2], rb * (8 * HEADS) + 16 * (h // 2 + 1))
                S.activation(den[:, h % 2, :].rearrange("p (a b) -> p a b", a=2), PS[DK:DK + 1, b0:b0 + 2, 0:ROWB],
                             ACT.Copy).then_inc(y_made, 1)

            with act.Fori(0, 2) as rb:
                for n in range(HEADS * NT):
                    h, j = divmod(n, NT)
                    u = rb * (HEADS * NT) + n
                    act.wait_ge(st_done, u + 1)
                    act.wait_ge(p_made, u + 1)
                    b0 = 2 * (n % 2)
                    S.activation(ER[:, n % 2, :].rearrange("p (a b) -> p a b", a=2), PS[:, b0:b0 + 2, 0:ROWB],
                                 ACT.Exp, scale=DK ** -0.5).then_inc(e_made, 1)
                    if j == 3 and h >= 1:
                        head_out(rb, h - 1)
                head_out(rb, HEADS - 1)
            for i in range(NT):
                deviation(4, i)

        @block.tensor
        def _(pe):
            T = nc.tensor
            pe.wait_ge(const, CONST)
            pe.wait_ge(ready, 1)
            T.matmul(mm_out(0, 4 * HALF, TT), ones[0:HALF, 0:TT], diag4[0:HALF, :, :].rearrange("p a b -> p (a b)"),
                     start=True, stop=True).then_inc(ext_t, 1)
            pe.wait_ge(ready, 2)
            T.transpose(mm_out(1, EC, HEADS), bmax[0:EC, :], ident[0:EC, 0:EC]).then_inc(ext_t, 1)
            pe.wait_ge(ready, 4)
            T.matmul(mm_out(2, HEADS, EC), ones[0:HEADS, 0:EC], diag8[0:HEADS, :], start=True, stop=True).then_inc(
                ext_t, 1)
            pe.wait_ge(ready, 5)
            T.matmul(mm_out(3, 1, TT), upper[0:TT, :], visits[0:TT, :], start=True, stop=True).then_inc(ext_t, 1)
            pe.sem_inc(hot_used, CH + HOTS)
            pe.wait_ge(ps_zero, 1)
            pe.wait_ge(ready, 6)
            pe.wait_ge(tab_in, 16)

            def build(rng, j, t4):
                lo, hi, off = rng
                pe.wait_ge(staged[(j + 2) % 4], t4 + (2 if j >= 2 else 1))

                def visit(c, first):
                    v = c + off
                    pe.wait_ge(hot_made, v + 1)
                    for q, part in enumerate((ownH, ownL)):
                        for b, (p0, p1) in enumerate(PIECES):
                            ins = T.matmul(mm_out(3 * (j % 2) + b, p1 - p0, (MH, MB)[q]),
                                           flat(part[0:EC, bass.ds(c, 1), :]),
                                           flat(hot[0:EC, bass.ds(v & (HOTS - 1), 1), p0:p1]),
                                           start=first and q == 0, stop=True, skip_group_check=True)
                    ins.then_inc(hot_used, 1)

                visit(lo, True)
                with pe.Fori(lo + 1, hi) as c:
                    visit(c, False)

            def mix(layer, h, n):
                pe.wait_ge(basis_in[h], n * 16 + 16)
                pe.wait_ge(w_copied, n * 2 + 1)
                for c in range(4):
                    ins = T.matmul(PS[32 * c:32 * c + RELS * FT, 6 + h, :],
                                   attbd[0:BJ, layer, :, :].rearrange("p r j -> p (r j)"),
                                   basis[0:BJ, h, c, :], start=True, stop=True, skip_group_check=True)
                ins.then_inc(w_done, 1)

            pe.wait_ge(ownb_made, 2)
            pe.wait_ge(owna_made, 1)
            for layer in range(2):
                with pe.Fori(16 * layer, 16 * layer + 16) as t4:
                    rngs = tile_ranges(pe, t4)
                    for j in range(4):
                        build(rngs[j], j, t4)
                        if j % 2:
                            mix(layer, j // 2, t4)
            pe.sem_inc(a_built, 1)

            def aggregate(s):
                with pe.Fori(0, NROWB) as rb:
                    cols = bass.ds(rb * ROWB, ROWB)
                    if s == 3:
                        pe.wait_ge(t_made, rb + 1)
                    for g in range(GROUPS[s]):
                        r, f = divmod(g, FT)
                        pe.wait_ge(agg_free, rb * GROUPS[s] + (AGG0[s] + g + 1))
                        fs = slice(f * P, (f + 1) * P)
                        for k in range(NT):
                            rel = r if s < 3 else 1
                            if f == 0:
                                pe.wait_ge(hi_made, PARTS0[s] + r * NT + k + 1)
                                pe.wait_ge(lo_made, PARTS0[s] + r * NT + k + 1)
                            for q in range(2):
                                ins = T.matmul(mm_out(g % 4, ROWB), GX[:, r, q, k, fs], CT[:, rel, k, cols],
                                               start=k == 0 and q == 0, stop=k == NT - 1 and q == 1)
                        ins.then_inc(agg_done, 1)
                    if s == 3:
                        for k in range(NT):
                            for q in range(2):
                                ins = T.matmul(PS[0:1, 4, 0:ROWB], dis16[:, q, k:k + 1], CT[:, 1, k, cols],
                                               start=k == 0 and q == 0, stop=k == NT - 1 and q == 1)
                        ins.then_inc(deg_done, 1)

            def project(s, i):
                if s == 4 or i >= 2:
                    pe.wait_ge(x_made, max(s * NT, s * NT + i - 1))
                rows = slice(i * P, (i + 1) * P)
                terms = []
                if s == 0:
                    terms = [(A16[:, p, k, rows], SUP[:, q, k, :]) for p, q in THREE for k in range(NT)]
                elif s == 4:
                    terms = [(yT[:, f, rows], W[:, 1, f, :]) for f in range(FT)]
                else:
                    for r in range(RELS_OF[s]):
                        terms += [(YT[:, r, p, f, rows], W16[:, r, q, f, :]) for p, q in THREE for f in range(FT)]
                    if s in (1, 2):
                        terms += [(XT16[:, p, f, rows], W16[:, 2, q, f, :]) for p, q in THREE for f in range(FT)]
                terms.append((trow[:, rows] if s == 3 else ones[0:1, :], brow[:, :]))
                for n, (lhs, rhs) in enumerate(terms):
                    ins = T.matmul(mm_out(4 + i % 2, D), lhs, rhs, start=n == 0, stop=n == len(terms) - 1)
                ins.then_inc(z_done, 1)

            def turn(s, n, i):
                if s >= 0:
                    pe.wait_ge(x_made, s * NT + i + 1)
                if n + i >= 2:
                    pe.wait_ge(xt_made, n + i - 1)
                for f in range(FT):
                    ins = T.transpose(PS[:, 6 + i % 2, f * P:(f + 1) * P], X[:, i, f * P:(f + 1) * P], ident[:, :])
                ins.then_inc(xt_done, 1)

            def gates(layer, i):
                pe.wait_ge(xt_made, NT * (layer + 1) + i + 1)
                for n, (p, q) in enumerate(THREE):
                    for f in range(FT):
                        ins = T.matmul(PS[:, 0, RELS * i:RELS * (i + 1)], XT16[:, p, f, i * P:(i + 1) * P],
                                       gw16[:, q, layer, f, :], start=n == 0 and f == 0, stop=n == 2 and f == FT - 1)
                ins.then_inc(gate_done, 1)

            pe.sem_inc(agg_free, 4)
            for j in (2, 3):
                pe.wait_ge(staged[j], TT // 4 + 1)
            pe.wait_ge(w_copied, TT // 2 + 1)
            for i in range(NT + 2):
                if i < NT:
                    pe.wait_ge(x_in[i // 3], 16)
                    turn(-1, 0, i)
                if i >= 2:
                    if i == 2:
                        pe.wait_ge(wgt_in, 16)
                    pe.wait_ge(xt_made, i - 1)
                    if i >= 6:
                        pe.wait_ge(sup_made, i - 5)
                    rows = slice((i - 2) * P, (i - 1) * P)
                    for f in range(FT):
                        ins = T.matmul(mm_out(i % 4, D), XT[:, f, rows], W[:, 0, f, :], start=f == 0,
                                       stop=f == FT - 1)
                    ins.then_inc(sup_done, 1)
            pe.wait_ge(bias_in, 16)
            pe.wait_ge(sup_made, NT)
            pe.wait_ge(a0_made, NT)
            for i in range(NT + 3):
                if i < NT:
                    project(0, i)
                if 2 <= i < NT + 2:
                    turn(0, NT, i - 2)
                if i >= 3:
                    gates(0, i - 3)
            pe.wait_ge(ct_made, NT * RELS + 1)
            for layer in range(2):
                pe.wait_ge(gate_made, layer + 1)
                aggregate(1 + layer)
                pe.wait_ge(w16_made, 3 * (layer + 1))
                pe.wait_ge(bias_in, 16 * (layer + 2))
                pe.wait_ge(agg_free, AGG0[layer + 2] + 4)
                for i in range(NT + 3):
                    if i < NT:
                        project(1 + layer, i)
                    if 2 <= i < NT + 2 and layer == 0:
                        turn(1, 2 * NT, i - 2)
                    if i >= 3 and layer == 0:
                        gates(1, i - 3)
            pe.wait_ge(csum_made, 1)
            for i in range(NT):
                for k in range(NT):
                    ins = T.matmul(PS[:, 0, i:i + 1], CT[:, 1, k, i * P:(i + 1) * P], one16[:, :], start=k == 0,
                                   stop=k == NT - 1)
            ins.then_inc(deg_done, 1)
            pe.wait_ge(s2, 1)
            aggregate(3)
            pe.wait_ge(w16_made, 7)
            pe.wait_ge(bias_in, 16 * 4)
            pe.wait_ge(agg_free, AGG0[4] + 4)
            pe.wait_ge(t_made, NROWB + 1)
            for i in range(NT + 2):
                if i < NT:
                    project(3, i)
                if i >= 2:
                    turn(3, 3 * NT, i - 2)
            pe.wait_ge(xt_made, 4 * NT)
            pe.wait_ge(w16_made, 9)
            pe.wait_ge(bias_in, 16 * 5)
            for g in range(2 * FT * 3):
                o_, which, p_ = g // 6, g // 3 % 2, g % 3
                lo, hi = PIECES[p_]
                if g >= 4:
                    pe.wait_ge(qkl_made, g - 3)
                for n, (p, q) in enumerate(THREE):
                    for f in range(FT):
                        ins = T.matmul(mm_out(g % 4, hi - lo), W16[:, 1 + which, q, f, o_ * P:(o_ + 1) * P],
                                       XT16[:, p, f, lo:hi], start=n == 0 and f == 0, stop=n == 2 and f == FT - 1)
                ins.then_inc(q_done, 1)

            def values(i, half):
                n = 2 * i + half
                if n:
                    pe.wait_ge(v_made, n)
                cols = slice(half * D // 2, (half + 1) * D // 2)
                for m, (p, q) in enumerate(THREE):
                    for f in range(FT):
                        T.matmul(PS[:, 7, 128:128 + D // 2], XT16[:, p, f, i * P:(i + 1) * P], W16[:, 0, q, f, cols],
                                 start=m == 0 and f == 0, stop=False)
                T.matmul(PS[:, 7, 128:128 + D // 2], ones[0:1, :], brow[:, cols], start=False,
                         stop=True).then_inc(v_done, 1)

            pe.wait_ge(w16_made, len(HALVED))
            pe.wait_ge(qkl_made, 2 * FT * 3)
            pe.wait_ge(qk_copied, 32 * FT)
            turned = PS[:, 6:8, :].rearrange("p a b -> p (a b)").bitcast(F16)
            for i in range(NT):
                if i >= 1:
                    pe.wait_ge(s_used, (i - 1) * HEADS + 1)
                    pe.wait_ge(v_made, 2 * i)
                for k in range(NT):
                    ins = T.transpose(turned[:, k * P:(k + 1) * P], CT[:, 0, k, i * P:(i + 1) * P], ident16[:, :])
                ins.then_inc(mt_done, 1)
                for h in range(HEADS):
                    idx = i * HEADS + h
                    if idx >= 2:
                        pe.wait_ge(s_used, idx - 1)
                    for b, (lo, hi) in enumerate(PIECES):
                        ins = T.matmul(mm_out(3 * (idx % 2) + b, hi - lo), QHH[:, h, i * P:(i + 1) * P],
                                       KHL[:, h, lo:hi], start=True, stop=True)
                    ins.then_inc(s_done, 1)
                    if h in (2, 5):
                        values(i, h // 3)
            pe.wait_ge(mxk_made, 1)
            T.transpose(mm_out(0, P, NT * HEADS), mxk, ident[:, :]).then_inc(mxt_done, 1)
            pe.sem_inc(pv_done, 4)
            pe.wait_ge(v_made, 2 * NT)
            pe.wait_ge(mrow_in, 16)
            pe.wait_ge(pool_made, 2)
            pe.wait_ge(mx_made, 1)

            def scores(rb, n):
                h, j = divmod(n, NT)
                pe.wait_ge(e_made, rb * (HEADS * NT) + (n + 1))
                for k, (key, query) in enumerate(((KHL, QHH), (KH, QL))):
                    for b in range(2):
                        ins = T.matmul(mm_out(2 * (n % 2) + b, ROWB), key[:, h, j * P:(j + 1) * P],
                                       query[:, h, bass.ds(rb * HB + b * ROWB, ROWB)], start=k == 0, stop=k == 1)
                ins.then_inc(st_done, 1)

            with pe.Fori(0, 2) as rb:
                scores(rb, 0)
                scores(rb, 1)
                for n in range(HEADS * NT):
                    h, j = divmod(n, NT)
                    if n + 2 < HEADS * NT:
                        scores(rb, n + 2)
                    if j == 0:
                        pe.wait_ge(y_made, rb * (2 * HEADS) + (2 * h + 2))
                    pe.wait_ge(p_made, rb * (HEADS * NT) + (n + 3))
                    for b in range(2):
                        ins = T.matmul(PS[0:DK + 1, 4 + 2 * (h % 2) + b, 0:ROWB], VA[:, j, h, :],
                                       BR[:, n % 4, b * ROWB:(b + 1) * ROWB], start=j == 0, stop=j == NT - 1)
                    ins.then_inc(pv_done, 1)
            pe.wait_ge(yn_made, 2 * HEADS + 2)
            pe.wait_ge(wgt_in, 16 * 8)
            pe.wait_ge(bias_in, 16 * 6)
            for i in range(NT):
                project(4, i)


def kernel(**inputs):
    import numpy as np
    import concourse.bacc as bacc
    from concourse.bass_utils import run_bass_kernel_spmd

    nc = bacc.Bacc("TRN2", target_bir_lowering=False, num_devices=1)
    i = {k: np.asarray(v) for k, v in inputs.items()}
    laid = {
        "x": i["x"],
        "src_t": i["src"].reshape(CH, EC).T,
        "dst_t": i["dst"].reshape(CH, EC).T,
        "dst_c": i["dst"].reshape(CH, EC),
        "type_t": i["edge_type_2"].reshape(CH, EC).T,
        "weight_t": i["edge_weight"].reshape(CH, EC).T,
        "attr_t": i["edge_attr_8"].reshape(CH, EC, HEADS).transpose(1, 0, 2),
        "W0": i["L0_gnn_weight"],
        "b0": i["L0_gnn_bias"],
        "W2": i["L2_gnn_W"].T,
        "b2": i["L2_gnn_b"],
        "bq_t": i["L3_gnn_bq"].reshape(HEADS, DK).T,
        "bk_t": i["L3_gnn_bk"].reshape(HEADS, DK).T,
        "bv": i["L3_gnn_bv"],
        "bo": i["L3_gnn_bo"],
    }
    for n in "qkvo":
        laid[f"W{n}"] = i[f"L3_gnn_W{n}"]
    for n in (1, 2):
        laid[f"basis{n}"] = i[f"L1_gnn_basis{n}"]
        laid[f"att{n}_r"] = np.repeat(i[f"L1_gnn_att{n}"].T, FT, axis=0)
        laid[f"gate_w{n}_t"] = i[f"L1_gnn_gate_w{n}"].reshape(RELS, FT, P).transpose(2, 1, 0).reshape(P, FT * RELS)
        laid[f"root{n}"] = i[f"L1_gnn_root{n}"]
        laid[f"bias{n}"] = i[f"L1_gnn_bias{n}"]
    arrays, aps = {}, {}
    for name, v in laid.items():
        arrays[f"in_{name}"] = np.ascontiguousarray(v)
        aps[name] = nc.dram_tensor(f"in_{name}", v.shape, mybir.dt.from_np(v.dtype), kind="ExternalInput").ap()
    out = nc.dram_tensor("out", (NODES, D), F32, kind="ExternalOutput").ap()
    gnn_resnorm(nc, aps, out)
    r = run_bass_kernel_spmd(nc, [arrays], core_ids=[0])
    return r.results[0]["out"]
```
